# Optimizing a Trainium2 kernel written in Bass

```python
import numpy as np
import jax
import jax.numpy as jnp

def _softmax(x, axis=-1):
    return jax.nn.softmax(x, axis=axis)

def _gelu(x):
    return jax.nn.gelu(x, approximate=True)

def _silu(x):
    return jax.nn.silu(x)

def _sigmoid(x):
    return jax.nn.sigmoid(x)

def _layernorm(x, axis=-1, eps=1e-05):
    m = jnp.mean(x, axis=axis, keepdims=True)
    v = jnp.var(x, axis=axis, keepdims=True)
    return (x - m) / jnp.sqrt(v + eps)

def _scatter_add(tgt, idx, src, axis=0):
    return tgt.at[idx].add(src)

def _segment_sum(src, seg, n):
    return jax.ops.segment_sum(src, seg, n)
kernel_name = 'mk_seq_postln_d1_jaxref_r4_c2d5fe'

def setup_inputs(seed: int=0):
    np.random.seed(seed)
    _w = jnp.asarray

    def _L0_attn_setup():
        import jax, jax.numpy as jnp
        import numpy as np
        N_HEADS = 16
        EPS = 1e-06

        def _phi(x):
            return jax.nn.softplus(x) + EPS

        def _reference_tuple_inner(x, Wq, Wk, Wv, Wo):
            B, T, D = x.shape
            H = N_HEADS
            dh = D // H

            def proj(W):
                y = jnp.einsum('btd,ed->bte', x, W)
                return y.reshape(B, T, H, dh).transpose(1, 0, 2, 3)
            q = proj(Wq)
            k = proj(Wk)
            v = proj(Wv)
            qf = _phi(q)
            kf = _phi(k)
            kv0 = jnp.zeros((B, H, dh, dh), dtype=x.dtype)
            z0 = jnp.zeros((B, H, dh), dtype=x.dtype)

            def step(carry, inp):
                kv, z = carry
                qt, kt, vt = inp
                kv = kv + jnp.einsum('bhd,bhe->bhde', kt, vt)
                z = z + kt
                num = jnp.einsum('bhd,bhde->bhe', qt, kv)
                den = jnp.einsum('bhd,bhd->bh', qt, z) + EPS
                return ((kv, z), num / den[..., None])
            (kv_acc, z_acc), out_t = jax.lax.scan(step, (kv0, z0), (qf, kf, v))
            out = out_t.transpose(1, 0, 2, 3).reshape(B, T, D)
            out = jnp.einsum('btd,ed->bte', out, Wo)
            return (out, kv_acc, z_acc)
        key = jax.random.key(seed)
        ks = jax.random.split(key, 5)
        D = 256
        s = 1.0 / np.sqrt(D)
        x = jax.random.normal(ks[0], (4, 1024, D), dtype=jnp.float32)
        Wq = jax.random.normal(ks[1], (D, D), dtype=jnp.float32) * s
        Wk = jax.random.normal(ks[2], (D, D), dtype=jnp.float32) * s
        Wv = jax.random.normal(ks[3], (D, D), dtype=jnp.float32) * s
        Wo = jax.random.normal(ks[4], (D, D), dtype=jnp.float32) * s
        return {'x': x, 'Wq': Wq, 'Wk': Wk, 'Wv': Wv, 'Wo': Wo}
    _L0_attn_in = _L0_attn_setup()

    def _L0_ffn_setup():
        import jax, jax.numpy as jnp
        import numpy as np
        import math
        D_IN = 256
        FEATURES = (1024, 1024, 256)
        BATCH, SEQ = (8, 512)

        def _conn_dense(kernel_bool, x):
            w = jnp.where(kernel_bool, jnp.float32(1.0), jnp.float32(-1.0))
            return x @ w
        key = jax.random.key(seed)
        kx, kk0, kk1, kk2 = jax.random.split(key, 4)
        x = jax.random.normal(kx, (BATCH, SEQ, D_IN), dtype=jnp.float32)
        k0 = jax.random.randint(kk0, (2 * D_IN, FEATURES[0]), 0, 2).astype(jnp.bool_)
        k1 = jax.random.randint(kk1, (FEATURES[0], FEATURES[1]), 0, 2).astype(jnp.bool_)
        k2 = jax.random.randint(kk2, (FEATURES[1], FEATURES[2]), 0, 2).astype(jnp.bool_)
        s0 = jnp.asarray(1.0 / math.sqrt(2 * D_IN), dtype=jnp.float32)
        s1 = jnp.asarray(1.0 / math.sqrt(FEATURES[0]), dtype=jnp.float32)
        s2 = jnp.asarray(1.0 / math.sqrt(FEATURES[1]), dtype=jnp.float32)
        return {'x': x, 'k0': k0, 'k1': k1, 'k2': k2, 's0': s0, 's1': s1, 's2': s2}
    _L0_ffn_in = _L0_ffn_setup()
    _d = {'L0_attn_x': _L0_attn_in['x'], 'L0_attn_Wq': _L0_attn_in['Wq'], 'L0_attn_Wk': _L0_attn_in['Wk'], 'L0_attn_Wv': _L0_attn_in['Wv'], 'L0_attn_Wo': _L0_attn_in['Wo'], 'L0_ffn_k0': _L0_ffn_in['k0'], 'L0_ffn_k1': _L0_ffn_in['k1'], 'L0_ffn_k2': _L0_ffn_in['k2'], 'L0_ffn_s0': _L0_ffn_in['s0'], 'L0_ffn_s1': _L0_ffn_in['s1'], 'L0_ffn_s2': _L0_ffn_in['s2']}
    _x0 = _d['L0_attn_x']
    _d['L0_attn_x'] = jax.random.normal(jax.random.fold_in(jax.random.key(seed), 1), (16, 512, 256), dtype=_x0.dtype)
    del _x0
    return _d

def reference(L0_attn_x, L0_attn_Wq, L0_attn_Wk, L0_attn_Wv, L0_attn_Wo, L0_ffn_k0, L0_ffn_k1, L0_ffn_k2, L0_ffn_s0, L0_ffn_s1, L0_ffn_s2):

    def _L0_attn_ref(x, Wq, Wk, Wv, Wo):
        import jax, jax.numpy as jnp
        import numpy as np
        N_HEADS = 16
        EPS = 1e-06

        def _phi(x):
            return jax.nn.softplus(x) + EPS

        def _reference_tuple_inner(x, Wq, Wk, Wv, Wo):
            B, T, D = x.shape
            H = N_HEADS
            dh = D // H

            def proj(W):
                y = jnp.einsum('btd,ed->bte', x, W)
                return y.reshape(B, T, H, dh).transpose(1, 0, 2, 3)
            q = proj(Wq)
            k = proj(Wk)
            v = proj(Wv)
            qf = _phi(q)
            kf = _phi(k)
            kv0 = jnp.zeros((B, H, dh, dh), dtype=x.dtype)
            z0 = jnp.zeros((B, H, dh), dtype=x.dtype)

            def step(carry, inp):
                kv, z = carry
                qt, kt, vt = inp
                kv = kv + jnp.einsum('bhd,bhe->bhde', kt, vt)
                z = z + kt
                num = jnp.einsum('bhd,bhde->bhe', qt, kv)
                den = jnp.einsum('bhd,bhd->bh', qt, z) + EPS
                return ((kv, z), num / den[..., None])
            (kv_acc, z_acc), out_t = jax.lax.scan(step, (kv0, z0), (qf, kf, v))
            out = out_t.transpose(1, 0, 2, 3).reshape(B, T, D)
            out = jnp.einsum('btd,ed->bte', out, Wo)
            return (out, kv_acc, z_acc)
        return _reference_tuple_inner(x, Wq, Wk, Wv, Wo)[0]

    def _L0_ffn_ref(x, k0, k1, k2, s0, s1, s2):
        import jax, jax.numpy as jnp
        import numpy as np
        import math
        D_IN = 256
        FEATURES = (1024, 1024, 256)
        BATCH, SEQ = (8, 512)

        def _conn_dense(kernel_bool, x):
            w = jnp.where(kernel_bool, jnp.float32(1.0), jnp.float32(-1.0))
            return x @ w
        h = jnp.concatenate([x, -x], axis=-1)
        h = s0 * _conn_dense(k0, h)
        h = jax.nn.relu(h) * 2
        h = s1 * _conn_dense(k1, h)
        h = jax.nn.relu(h) * 2
        h = s2 * _conn_dense(k2, h)
        return h
    x = L0_attn_x
    x = _layernorm(x + _L0_attn_ref(x, L0_attn_Wq, L0_attn_Wk, L0_attn_Wv, L0_attn_Wo), axis=-1)
    x = _layernorm(x + _L0_ffn_ref(x, L0_ffn_k0, L0_ffn_k1, L0_ffn_k2, L0_ffn_s0, L0_ffn_s1, L0_ffn_s2), axis=-1)
    return x

_drawn_inputs = setup_inputs


def setup_inputs(seed=0):
    import zlib

    import numpy as np

    out = dict(_drawn_inputs(seed))
    spreads = {}
    factors = {'L0_attn_Wq': 4.905}
    for name, (base, spread) in spreads.items():
        noise = np.random.default_rng([zlib.crc32(name.encode()), seed]).standard_normal(out[name].shape)
        drawn = base * np.exp(spread * noise) if base else spread * noise
        out[name] = jnp.asarray(drawn.astype(out[name].dtype))
    for name, factor in factors.items():
        out[name] = (out[name] * factor).astype(out[name].dtype)
    return out
```

```python
from contextlib import ExitStack

import numpy as np

import concourse.bass as bass
from concourse import mybir
from concourse.alu_op_type import AluOpType as ALU

ACT = mybir.ActivationFunctionType
F32 = mybir.dt.float32
F16 = mybir.dt.float16
U8 = mybir.dt.uint8

P = 128
B, T, D = 16, 512, 256
H = 16
DH = D // H
C = T // P
G = D // P
PAIRS = P // (2 * DH)
F = 1024
FT = F // P
PHI_EPS = 1e-6
LN_EPS = 1e-5
CLAMP = 18.0
X_SCALE = 2.0 ** 11
H1_SCALE = 2.0 ** 6
H2_SCALE = 2.0 ** -4
ATT_JOBS = 14
FFN_JOBS = 22
CONST_IN = 5 * 16


class Tally:

    def __init__(self, sem, per_sequence):
        self.sem, self.per = sem, per_sequence

    def at(self, b, n):
        return b * self.per + n


def layer_kernel(nc, x, x_t, wq_t, wk_t, wv_t, wo_t, k0, k1, k2, s_in, causal_in, blocks_in, parity_in,
                 ident_in, out):
    x_rows = x.rearrange("b (c p) d -> b p c d", p=P)
    out_rows = out.rearrange("b (c p) d -> b p c d", p=P)
    xt_rows = x_t.rearrange("b (g p) t -> b p g t", p=P)

    ctx = ExitStack()
    with ctx:
        def sb(name, shape, dt=F32):
            return ctx.enter_context(nc.sbuf_tensor(name, shape, dt))

        def sem(name):
            return ctx.enter_context(nc.semaphore(name))

        def tally(name, per):
            return Tally(sem(name), per)

        wq, wk, wv, wo = (sb(n, [P, G, D]) for n in ("wq", "wk", "wv", "wo"))
        causal = sb("causal", [P, P])
        blocks = sb("blocks", [P, P])
        parity = sb("parity", [P, 2])
        ident = sb("ident", [P, P])
        ident16 = sb("ident16", [P, P], F16)
        k0_raw = sb("k0_raw", [P, 2 * G, F], U8)
        k1_raw = sb("k1_raw", [P, FT, F], U8)
        k2_raw = sb("k2_raw", [P, FT, D], U8)
        w0 = sb("w0", [P, G, F], F16)
        w1 = sb("w1", [P, FT, F], F16)
        w2 = sb("w2", [P, FT, D], F16)
        s_raw = sb("s_raw", [P, 3])
        s_neg = sb("s_neg", [P, 3])
        s_sign = sb("s_sign", [P, 3])
        s_abs = sb("s_abs", [P, 3])
        c0 = sb("c0", [P, 1])
        c1 = sb("c1", [P, 2])
        out_scale = sb("out_scale", [P, 2])
        phi_eps = sb("phi_eps", [P, 1])
        consts = sb("consts", [P, 2])
        xt_sb = sb("xt_sb", [P, G, T])
        x_sb = sb("x_sb", [P, C, D])
        soft = sb("soft", [P, 2, T])
        qf = sb("qf", [P, G, T])
        kf = sb("kf", [P, G, T])
        q_par = sb("q_par", [P, 2, G, T])
        zc = sb("zc", [P, G, T])
        qz = sb("qz", [P, G, T])
        vpad = sb("vpad", [P, C, H // 2, 4 * DH])
        k_tok = sb("k_tok", [P, C - 1, D])
        s_sb = sb("s_sb", [P, PAIRS, 2 * G, P])
        kv_sb = sb("kv_sb", [P, G, P])
        den = sb("den", [P, G, T])
        rden = sb("rden", [P, G, T])
        attn = sb("attn", [P, G, P])
        r1 = sb("r1", [P, C, D])
        st1 = sb("st1", [P, 7])
        mv1 = sb("mv1", [P, C, 2])
        rs1 = sb("rs1", [P, C, 2])
        x1 = sb("x1", [P, C, D])
        x1h = sb("x1h", [P, C, D], F16)
        x1l = sb("x1l", [P, C, D], F16)
        x1_keep = sb("x1_keep", [P, C, D])
        x1t = sb("x1t", [P, 2, G, T], F16)
        h1 = sb("h1", [P, 2, FT, T], F16)
        h2 = sb("h2", [P, 2, FT, T], F16)
        r2 = sb("r2", [P, C, D])
        st2 = sb("st2", [P, 7])
        mv2 = sb("mv2", [P, C, 2])
        rs2 = sb("rs2", [P, C, 2])
        y = sb("y", [P, C, D])

        def bank(name):
            return ctx.enter_context(nc.psum_tensor(name, [P, 512], F32))

        ffn_ps = [bank("ffn_ps0"), bank("ffn_ps1")]
        att_ps = [bank("att_ps0"), bank("att_ps1")]
        s_ps = [bank("s_ps0"), bank("s_ps1")]
        h1_ps = ffn_ps + s_ps
        num_ps = bank("num_ps")
        kv_ps = bank("kv_ps")
        num_v = num_ps[:, 0:G * P].rearrange("p (g t) -> p g t", g=G)
        kv_v = kv_ps[:, 0:G * P].rearrange("p (g t) -> p g t", g=G)

        wk_in, wq_in, wvo_in = sem("wk_in"), sem("wq_in"), sem("wvo_in")
        const_in, k0_in, k1_in, k2_in = sem("const_in"), sem("k0_in"), sem("k1_in"), sem("k2_in")
        scal = sem("scal")
        lnc_ready = sem("lnc_ready")
        zeroed = sem("zeroed")
        w0_ready, w12_ready = sem("w0_ready"), sem("w12_ready")
        xt_in = tally("xt_in", 16)
        x_in = [tally(f"x_in{c}", 16) for c in range(C)]
        y_out = [tally(f"y_out{c}", 16) for c in range(C)]
        att_full = tally("att_full", ATT_JOBS)
        clamped = tally("clamped", 4)
        exped = tally("exped", 4)
        logged = tally("logged", 4)
        feat = tally("feat", 4)
        scanned = tally("scanned", G)
        q_split = tally("q_split", G)
        qz_ready = tally("qz_ready", G)
        v_ready = tally("v_ready", C)
        kt_ready = tally("kt_ready", C - 1)
        s_full = tally("s_full", C * PAIRS)
        s_done = tally("s_done", C * PAIRS)
        num_full = tally("num_full", C)
        kv_full = tally("kv_full", C - 1)
        kv_ready = tally("kv_ready", C - 1)
        den_ready = tally("den_ready", G)
        rden_ready = tally("rden_ready", C)
        attn_ready = tally("attn_ready", C)
        ln1_sum = tally("ln1_sum", C)
        ln1_step = tally("ln1_step", 2 * C)
        ln1_stat = tally("ln1_stat", 2 * C)
        x1_ready = tally("x1_ready", C)
        x1h_ready = tally("x1h_ready", C)
        x1l_ready = tally("x1l_ready", C)
        ffn_full = tally("ffn_full", FFN_JOBS)
        x1_kept = tally("x1_kept", 1)
        x1t_ready = [tally(f"x1t_ready{i}", 1) for i in range(2)]
        high_ready = tally("high_ready", 2 * FT)
        low_ready = tally("low_ready", 2 * FT)
        ln2_sum = tally("ln2_sum", C)
        ln2_step = tally("ln2_step", 2 * C)
        ln2_stat = tally("ln2_stat", 2 * C)
        y_ready = tally("y_ready", C)

        block = ctx.enter_context(nc.Block())

        @block.sync
        def _(sp):
            def load_x(b):
                sp.dma_start(xt_sb[:], xt_rows[b]).then_inc(xt_in.sem, 16)

            def load_rows(b, c):
                sp.dma_start(x_sb[:, c, :], x_rows[b, :, c, :]).then_inc(x_in[c].sem, 16)

            def reload(b):
                sp.wait_ge(att_full.sem, att_full.at(b - 1, 6))
                load_x(b)
                for c in range(C):
                    sp.wait_ge(ln1_sum.sem, ln1_sum.at(b - 1, c + 1))
                    load_rows(b, c)

            def store(f):
                for c in range(C):
                    sp.wait_ge(y_ready.sem, y_ready.at(f, c + 1))
                    sp.dma_start(out_rows[f, :, c, :], y[:, c, :]).then_inc(y_out[c].sem, 16)

            sp.dma_start(wk[:], wk_t.rearrange("(g p) n -> p g n", p=P)).then_inc(wk_in, 16)
            load_x(0)
            sp.dma_start(wq[:], wq_t.rearrange("(g p) n -> p g n", p=P)).then_inc(wq_in, 16)
            sp.dma_start(wv[:], wv_t.rearrange("(g p) n -> p g n", p=P)).then_inc(wvo_in, 16)
            sp.dma_start(wo[:], wo_t.rearrange("(g p) n -> p g n", p=P)).then_inc(wvo_in, 16)
            for c in range(C):
                load_rows(0, c)
            sp.dma_start(k0_raw[:], k0.rearrange("(g p) n -> p g n", p=P)).then_inc(k0_in, 16)
            sp.dma_start(k1_raw[:], k1.rearrange("(g p) n -> p g n", p=P)).then_inc(k1_in, 16)
            sp.dma_start(k2_raw[:], k2.rearrange("(g p) n -> p g n", p=P)).then_inc(k2_in, 16)
            reload(1)
            with sp.Fori(0, B - 2) as f:
                reload(f + 2)
                store(f)
            store(B - 2)
            store(B - 1)
            for c in range(C):
                sp.wait_ge(y_out[c].sem, y_out[c].at(B, 16))

        @block.tensor
        def _(pe):
            def att_bank(b, n, first=False):
                if n >= 12:
                    pe.wait_ge(ln1_sum.sem, ln1_sum.at(b, n - 11))
                elif n >= 10:
                    pe.wait_ge(den_ready.sem, den_ready.at(b, n - 9))
                elif n >= 8:
                    pe.wait_ge(kt_ready.sem, kt_ready.at(b, n - 6))
                elif n >= 4:
                    pe.wait_ge(feat.sem, feat.at(b, n - 3))
                elif n >= 2:
                    pe.wait_ge(v_ready.sem, v_ready.at(b, 2 * (n - 1)))
                elif not first:
                    pe.wait_ge(ln1_sum.sem, ln1_sum.at(b - 1, C - 1 + n))
                return att_ps[n % 2]

            def hidden1_bank(f, m):
                if m < 2:
                    pe.wait_ge(x1t_ready[m].sem, x1t_ready[m].at(f, 1))
                elif m < 4:
                    pe.wait_ge(s_done.sem, s_done.at(f, C * PAIRS + 2))
                else:
                    pe.wait_ge(low_ready.sem, low_ready.at(f, m - 3))
                return h1_ps[m % 4]

            def ffn_bank(f, n):
                if n >= 4 + 2 * FT:
                    pe.wait_ge(ln2_sum.sem, ln2_sum.at(f, C + n - 3 - 2 * FT))
                elif n >= 4 + FT:
                    pe.wait_ge(low_ready.sem, low_ready.at(f, n - 3))
                elif n >= 2 + FT:
                    pe.wait_ge(low_ready.sem, low_ready.at(f, n - 5))
                else:
                    pe.wait_ge(ln2_sum.sem, ln2_sum.at(f, C - 1 + n))
                return ffn_ps[n % 2]

            def project(b, n, w, g):
                ps = att_bank(b, n)
                for d in range(G):
                    mm = pe.matmul(ps[:], w[:, d, g * P:(g + 1) * P], xt_sb[:, d, :],
                                   start=(d == 0), stop=(d == G - 1))
                mm.then_inc(att_full.sem, 1)

            def project_v(b, half, first):
                ps = att_bank(b, half, first)
                for i in range(2):
                    c = 2 * half + i
                    for d in range(G):
                        mm = pe.matmul(ps[:, i * D:(i + 1) * D], xt_sb[:, d, c * P:(c + 1) * P], wv[:, d, :],
                                       start=(d == 0), stop=(d == G - 1))
                mm.then_inc(att_full.sem, 1)

            def transpose_k(b, n, chunks):
                ps = att_bank(b, n)
                pe.wait_ge(feat.sem, feat.at(b, 2))
                for i, c in enumerate(chunks):
                    for g in range(G):
                        mm = pe.transpose(ps[:, i * D + g * P:i * D + (g + 1) * P],
                                          kf[:, g, c * P:(c + 1) * P], ident[:])
                mm.then_inc(att_full.sem, 1)

            def scores(b, f, c, a):
                n = c * PAIRS + a
                if n >= 2:
                    pe.wait_ge(s_done.sem, s_done.at(b, n + 1))
                elif f is not None:
                    pe.wait_ge(low_ready.sem, low_ready.at(f, FT - 1 + n))
                pe.wait_ge(q_split.sem, q_split.at(b, G))
                ps = s_ps[a % 2]
                rows = slice(2 * DH * a, 2 * DH * (a + 1))
                for g in range(G):
                    mm = pe.matmul(ps[:, g * 2 * P:(g + 1) * 2 * P], kf[rows, g, c * P:(c + 1) * P],
                                   q_par[rows, :, g, c * P:(c + 1) * P], start=True, stop=True)
                mm.then_inc(s_full.sem, 1)

            def denominator(b, n, g):
                ps = att_bank(b, n)
                pe.wait_ge(qz_ready.sem, qz_ready.at(b, g + 1))
                pe.matmul(ps[:], blocks[:], qz[:, g, :], start=True, stop=True).then_inc(att_full.sem, 1)

            def weigh(b, c):
                if c > 0:
                    pe.wait_ge(kv_ready.sem, kv_ready.at(b, c))
                    for g in range(G):
                        pe.matmul(num_v[:, g, :], kv_sb[:, g, :], qf[:, g, c * P:(c + 1) * P],
                                  start=(g == 0), stop=False, skip_group_check=True)
                pe.wait_ge(v_ready.sem, v_ready.at(b, c + 1))
                pe.wait_ge(s_done.sem, s_done.at(b, (c + 1) * PAIRS + 2))
                for g in range(G):
                    for par in range(2):
                        for a in range(PAIRS):
                            pair = g * PAIRS + a
                            mm = pe.matmul(num_v[2 * DH * a:2 * DH * (a + 1), g, :],
                                           vpad[:, c, pair, par * 2 * DH:(par + 1) * 2 * DH],
                                           s_sb[:, a, 2 * g + par, :],
                                           start=(c == 0 and g == 0 and par == 0), stop=(par == 1),
                                           skip_group_check=True)
                mm.then_inc(num_full.sem, 1)
                if c < C - 1:
                    pe.wait_ge(kt_ready.sem, kt_ready.at(b, c + 1))
                    for g in range(G):
                        v = vpad[:, c, g * PAIRS:(g + 1) * PAIRS, :].rearrange(
                            "p a (q e) -> p a q e", e=DH)[:, :, 0:4:3, :]
                        mm = pe.matmul(kv_v[:, g, :], k_tok[:, c, g * P:(g + 1) * P], v,
                                       start=(c == 0 and g == 0), stop=True, skip_group_check=True)
                    mm.then_inc(kv_full.sem, 1)

            def project_out(b, c):
                ps = att_bank(b, 10 + c)
                pe.wait_ge(attn_ready.sem, attn_ready.at(b, c + 1))
                for g in range(G):
                    mm = pe.matmul(ps[:, 0:D], attn[:, g, :], wo[:, g, :],
                                   start=(g == 0), stop=(g == G - 1))
                mm.then_inc(att_full.sem, 1)

            def transpose_x1(f, half):
                ps = ffn_bank(f, half)[:].bitcast(F16).rearrange("p (c h g t) -> p c h g t", c=2, h=2, g=G)
                pe.wait_ge(x1l_ready.sem, x1l_ready.at(f, 2 * half + 2))
                for i in range(2):
                    for h, part in enumerate((x1h, x1l)):
                        for g in range(G):
                            mm = pe.transpose(ps[:, i, h, g, :],
                                              part[:, 2 * half + i, g * P:(g + 1) * P], ident16[:])
                mm.then_inc(ffn_full.sem, 1)

            def hidden1(f, m):
                ps = hidden1_bank(f, m)
                if m == 0:
                    pe.wait_ge(x1t_ready[0].sem, x1t_ready[0].at(f, 1))
                    pe.wait_ge(x1t_ready[1].sem, x1t_ready[1].at(f, 1))
                for d in range(G):
                    for h in range(2):
                        mm = pe.matmul(ps[:], w0[:, d, m * P:(m + 1) * P], x1t[:, h, d, :],
                                       start=(d == 0 and h == 0), stop=(d == G - 1 and h == 1))
                mm.then_inc(ffn_full.sem, 1)

            def hidden2(f, m, part=None):
                ps = ffn_ps[m % 2]
                if part != 1:
                    ffn_bank(f, 2 + FT + m)
                for d in range(FT) if part is None else range(part * FT // 2, (part + 1) * FT // 2):
                    if m == 0:
                        pe.wait_ge(low_ready.sem, low_ready.at(f, d + 1))
                    for h in range(2):
                        mm = pe.matmul(ps[:], w1[:, d, m * P:(m + 1) * P], h1[:, h, d, :],
                                       start=(d == 0 and h == 0), stop=(d == FT - 1 and h == 1))
                if part != 0:
                    mm.then_inc(ffn_full.sem, 1)

            def ffn_out(f, c):
                ps = ffn_bank(f, 2 + 2 * FT + c)
                for d in range(FT):
                    if c == 0:
                        pe.wait_ge(low_ready.sem, low_ready.at(f, FT + d + 1))
                    for h in range(2):
                        mm = pe.matmul(ps[:, 0:D], h2[:, h, d, c * P:(c + 1) * P], w2[:, d, :],
                                       start=(d == 0 and h == 0), stop=(d == FT - 1 and h == 1))
                mm.then_inc(ffn_full.sem, 1)

            def step(b, f):
                att, ffn = b is not None, f is not None
                if att:
                    pe.wait_ge(xt_in.sem, xt_in.at(b, 16))
                    project_v(b, 0, not ffn)
                    project_v(b, 1, not ffn)
                if ffn:
                    transpose_x1(f, 0)
                    transpose_x1(f, 1)
                if att:
                    project(b, 2, wk, 0)
                if ffn:
                    hidden1(f, 0)
                if att:
                    project(b, 3, wk, 1)
                if ffn:
                    hidden1(f, 1)
                    hidden1(f, 2)
                if att:
                    project(b, 4, wq, 0)
                if ffn:
                    hidden1(f, 3)
                    hidden1(f, 4)
                if att:
                    project(b, 5, wq, 1)
                if ffn:
                    hidden1(f, 5)
                if ffn:
                    hidden1(f, 6)
                    hidden1(f, 7)
                if ffn:
                    hidden2(f, 0)
                if att:
                    transpose_k(b, 6, (0, 1))
                    transpose_k(b, 7, (2,))
                for c in range(C):
                    last = c == C - 1
                    if att:
                        scores(b, f, c, 0)
                        scores(b, f, c, 1)
                    if ffn:
                        hidden2(f, 1 + 2 * c)
                    if att and c == 0:
                        denominator(b, 8, 0)
                        denominator(b, 9, 1)
                    if att:
                        scores(b, f, c, 2)
                        scores(b, f, c, 3)
                    if ffn:
                        ffn_out(f, 0) if last else hidden2(f, 2 + 2 * c, 0)
                    if att:
                        weigh(b, c)
                    if ffn:
                        ffn_out(f, 1) if last else hidden2(f, 2 + 2 * c, 1)
                    if att:
                        project_out(b, c)
                if ffn:
                    ffn_out(f, 2)
                    ffn_out(f, 3)

            pe.wait_ge(wvo_in, 32)
            pe.wait_ge(wk_in, 16)
            pe.wait_ge(wq_in, 16)
            pe.wait_ge(const_in, CONST_IN)
            pe.wait_ge(zeroed, 1)
            step(0, None)
            pe.wait_ge(scal, 8)
            pe.wait_ge(w0_ready, 2 + G)
            pe.wait_ge(w12_ready, 2 * FT)
            with pe.Fori(0, B - 1) as f:
                step(f + 1, f)
            step(None, B - 1)

        @block.scalar
        def _(act):
            def exp_log(b, n):
                s = soft[:, n % 2, :]
                act.wait_ge(clamped.sem, clamped.at(b, n + 1))
                act.activation(s, s, ACT.Exp).then_inc(exped.sem, 1)
                act.wait_ge(exped.sem, exped.at(b, n + 1))
                act.activation(s, s, ACT.Ln, bias=1.0).then_inc(logged.sem, 1)

            def pad_v(b, half):
                act.wait_ge(att_full.sem, att_full.at(b, half + 1))
                for i in range(2):
                    c = 2 * half + i
                    to = vpad[:, c, :, :].rearrange("p a (q e) -> p a q e", e=DH)[:, :, 0:4:3, :]
                    of = att_ps[half][:, i * D:(i + 1) * D].rearrange("p (a q e) -> p a q e", q=2, e=DH)
                    act.activation(to, of, ACT.Copy).then_inc(v_ready.sem, 1)

            def keep_k(b, n, chunks):
                act.wait_ge(att_full.sem, att_full.at(b, n + 1))
                for i, c in enumerate(chunks):
                    act.activation(k_tok[:, c, :], att_ps[n % 2][:, i * D:(i + 1) * D],
                                   ACT.Copy).then_inc(kt_ready.sem, 1)

            def denominator(b, g):
                act.wait_ge(att_full.sem, att_full.at(b, 9 + g))
                act.activation(den[:, g, :], att_ps[g][:], ACT.Identity, bias=phi_eps[:]).then_inc(den_ready.sem, 1)

            def high_x1(b, c):
                act.wait_ge(x1_ready.sem, x1_ready.at(b, c + 1))
                act.activation(x1h[:, c, :], x1[:, c, :], ACT.Copy, scale=X_SCALE).then_inc(x1h_ready.sem, 1)

            def keep_x1(f):
                act.wait_ge(x1_ready.sem, x1_ready.at(f, C))
                act.wait_ge(ln2_sum.sem, ln2_sum.at(f, C))
                act.activation(x1_keep[:], x1[:], ACT.Copy).then_inc(x1_kept.sem, 1)

            def keep_x1t(f):
                act.wait_ge(ffn_full.sem, ffn_full.at(f, 1))
                act.activation(x1t[:, :, :, 0:2 * P].rearrange("p h g (c t) -> p c (h g) t", c=2),
                               ffn_ps[0][:].bitcast(F16).rearrange("p (c h t) -> p c h t", c=2, h=2 * G),
                               ACT.Copy).then_inc(x1t_ready[0].sem, 1)

            def high(f, layer, m):
                n = layer * FT + m
                act.wait_ge(ffn_full.sem, ffn_full.at(f, 2 + n + 1))
                to, of = ((h1, h1_ps[m % 4]), (h2, ffn_ps[m % 2]))[layer]
                act.activation(to[:, 0, m, :], of[:], ACT.Relu).then_inc(high_ready.sem, 1)

            def step(b, f, prepare=lambda: None):
                att, ffn = b is not None, f is not None
                if att:
                    pad_v(b, 0)
                    pad_v(b, 1)
                if ffn:
                    keep_x1t(f)
                    keep_x1(f)
                if att:
                    exp_log(b, 0)
                if ffn:
                    high(f, 0, 0)
                if att:
                    exp_log(b, 1)
                if ffn:
                    high(f, 0, 1)
                    high(f, 0, 2)
                if att:
                    exp_log(b, 2)
                if ffn:
                    high(f, 0, 3)
                    high(f, 0, 4)
                if att:
                    exp_log(b, 3)
                if ffn:
                    high(f, 0, 5)
                if ffn:
                    high(f, 0, 6)
                    high(f, 0, 7)
                    high(f, 1, 0)
                if att:
                    keep_k(b, 6, (0, 1))
                    keep_k(b, 7, (2,))
                prepare()
                for c in range(C):
                    last = c == C - 1
                    if ffn:
                        high(f, 1, 1 + 2 * c)
                    if att and c == 0:
                        denominator(b, 0)
                        denominator(b, 1)
                    if ffn and not last:
                        high(f, 1, 2 + 2 * c)
                    if att:
                        high_x1(b, c)

            def signs():
                act.wait_ge(scal, 6)
                act.wait_ge(k1_in, 16)
                act.wait_ge(k2_in, 16)
                for d in range(FT):
                    act.activation(w1[:, d, :], k1_raw[:, d, :], ACT.Identity, bias=c1[:, 1:2],
                                   scale=c1[:, 0:1]).then_inc(w12_ready, 1)
                for d in range(FT):
                    act.activation(w2[:, d, :], k2_raw[:, d, :], ACT.Copy, bias=-1.0,
                                   scale=2.0).then_inc(w12_ready, 1)

            act.dma_start(parity[:], parity_in).then_inc(const_in, 16)
            act.dma_start(causal[:], causal_in).then_inc(const_in, 16)
            act.dma_start(blocks[:], blocks_in).then_inc(const_in, 16)
            act.dma_start(ident[:], ident_in).then_inc(const_in, 16)
            act.dma_start(s_raw[:], s_in).then_inc(const_in, 16)
            act.sem_inc(x1_kept.sem, 1)
            act.sem_inc(ln2_sum.sem, C)
            for c in range(C):
                act.sem_inc(y_out[c].sem, 16)
            act.preload_act_table_set("natural_log_exp_and_others")
            act.wait_ge(scal, 1)
            step(0, None, signs)
            with act.Fori(0, B - 1) as f:
                step(f + 1, f)
            step(None, B - 1)

        @block.vector
        def _(dve):
            def clamp(b, n):
                dve.wait_ge(att_full.sem, att_full.at(b, 2 + n + 1))
                dve.tensor_scalar(soft[:, n % 2, :], att_ps[n % 2][:], CLAMP, None,
                                  ALU.min).then_inc(clamped.sem, 1)

            def features(b, n):
                dve.wait_ge(logged.sem, logged.at(b, n + 1))
                to = (kf, qf)[n // 2][:, n % 2, :]
                dve.scalar_tensor_tensor(out=to, in0=soft[:, n % 2, :], scalar=PHI_EPS,
                                         in1=att_ps[n % 2][:], op0=ALU.add, op1=ALU.max).then_inc(feat.sem, 1)

            def prefix(b, g):
                dve.tensor_tensor_scan(out=zc[:, g, :], data0=kf[:, g, :], data1=kf[:, g, :], initial=0.0,
                                       op0=ALU.add, op1=ALU.bypass).then_inc(scanned.sem, 1)

            def mask_scores(b, c, a):
                n = c * PAIRS + a
                dve.wait_ge(s_full.sem, s_full.at(b, n + 1))
                dve.tensor_tensor(s_sb[:, a, :, :], s_ps[a % 2][:].rearrange("p (h t) -> p h t", t=P),
                                  causal[:].unsqueeze(1).to_broadcast([P, 2 * G, P]),
                                  ALU.mult).then_inc(s_done.sem, 1)

            def invert(b, c):
                dve.wait_ge(den_ready.sem, den_ready.at(b, G))
                dve.reciprocal(rden[:, :, c * P:(c + 1) * P],
                               den[:, :, c * P:(c + 1) * P]).then_inc(rden_ready.sem, 1)

            def divide(b, c):
                dve.wait_ge(rden_ready.sem, rden_ready.at(b, c + 1))
                dve.wait_ge(num_full.sem, num_full.at(b, c + 1))
                dve.tensor_tensor(attn[:], num_v, rden[:, :, c * P:(c + 1) * P], ALU.mult).then_inc(attn_ready.sem, 1)

            def keep_state(b, c):
                dve.wait_ge(kv_full.sem, kv_full.at(b, c + 1))
                dve.tensor_tensor(kv_sb[:], kv_v, blocks[:].unsqueeze(1).to_broadcast([P, G, P]),
                                  ALU.mult).then_inc(kv_ready.sem, 1)

            def statistics(b, c, r, st, mv, step_):
                dve.bn_stats(st[:, 0:6], r[:, c, :]).then_inc(step_.sem, 1)
                dve.wait_ge(step_.sem, step_.at(b, 2 * c + 1))
                dve.tensor_copy(st[:, 6:7], st[:, 0:1])
                dve.bn_aggr(mv[:, c, :], st[:, 0:6]).then_inc(step_.sem, 1)

            def norm1(b, c):
                n = 10 + c
                dve.wait_ge(att_full.sem, att_full.at(b, n + 1))
                dve.wait_ge(x_in[c].sem, x_in[c].at(b, 16))
                dve.tensor_tensor(r1[:, c, :], att_ps[n % 2][:, 0:D], x_sb[:, c, :],
                                  ALU.add).then_inc(ln1_sum.sem, 1)
                dve.wait_ge(ln1_sum.sem, ln1_sum.at(b, c + 1))
                statistics(b, c, r1, st1, mv1, ln1_step)

            def normalise1(b, c):
                dve.wait_ge(ln1_stat.sem, ln1_stat.at(b, 2 * c + 2))
                dve.wait_ge(x1_kept.sem, x1_kept.at(b, 1))
                dve.tensor_scalar(x1[:, c, :], r1[:, c, :], mv1[:, c, 0:1], rs1[:, c, 1:2], ALU.subtract,
                                  ALU.mult).then_inc(x1_ready.sem, 1)

            def normalise2(f, c):
                dve.wait_ge(ln2_stat.sem, ln2_stat.at(f, 2 * c + 2))
                dve.wait_ge(y_out[c].sem, y_out[c].at(f, 16))
                dve.tensor_scalar(y[:, c, :], r2[:, c, :], mv2[:, c, 0:1], rs2[:, c, 1:2], ALU.subtract,
                                  ALU.mult).then_inc(y_ready.sem, 1)

            def low_x1(b, c):
                dve.wait_ge(x1h_ready.sem, x1h_ready.at(b, c + 1))
                dve.scalar_tensor_tensor(out=x1l[:, c, :], in0=x1[:, c, :], scalar=X_SCALE,
                                         in1=x1h[:, c, :], op0=ALU.mult,
                                         op1=ALU.subtract).then_inc(x1l_ready.sem, 1)

            def keep_x1t(f):
                dve.wait_ge(ffn_full.sem, ffn_full.at(f, 2))
                dve.tensor_copy(x1t[:, :, :, 2 * P:4 * P].rearrange("p h g (c t) -> p c (h g) t", c=2),
                                ffn_ps[1][:].bitcast(F16).rearrange("p (c h t) -> p c h t", c=2, h=2 * G)
                                ).then_inc(x1t_ready[1].sem, 1)

            def low(f, layer, m):
                n = layer * FT + m
                to, of = ((h1, h1_ps[m % 4]), (h2, ffn_ps[m % 2]))[layer]
                dve.wait_ge(high_ready.sem, high_ready.at(f, n + 1))
                dve.scalar_tensor_tensor(out=to[:, 1, m, :], in0=of[:], scalar=0.0,
                                         in1=to[:, 0, m, :], op0=ALU.max,
                                         op1=ALU.subtract).then_inc(low_ready.sem, 1)

            def norm2(f, c):
                n = c
                dve.wait_ge(ffn_full.sem, ffn_full.at(f, 2 + 2 * FT + c + 1))
                dve.wait_ge(x1_kept.sem, x1_kept.at(f, 2))
                dve.scalar_tensor_tensor(out=r2[:, c, :], in0=ffn_ps[n % 2][:, 0:D], scalar=out_scale[:, 1:2],
                                         in1=x1_keep[:, c, :], op0=ALU.mult,
                                         op1=ALU.add).then_inc(ln2_sum.sem, 1)
                dve.wait_ge(ln2_sum.sem, ln2_sum.at(f, C + c + 1))
                statistics(f, c, r2, st2, mv2, ln2_step)

            def step(b, f, prepare=lambda: None):
                att, ffn = b is not None, f is not None
                if ffn:
                    keep_x1t(f)
                if att:
                    clamp(b, 0)
                if ffn:
                    low(f, 0, 0)
                if att:
                    features(b, 0)
                    clamp(b, 1)
                if ffn:
                    low(f, 0, 1)
                if att:
                    features(b, 1)
                if ffn:
                    low(f, 0, 2)
                if att:
                    clamp(b, 2)
                    prefix(b, 0)
                if ffn:
                    low(f, 0, 3)
                if att:
                    features(b, 2)
                if ffn:
                    low(f, 0, 4)
                if att:
                    clamp(b, 3)
                    prefix(b, 1)
                if ffn:
                    low(f, 0, 5)
                if att:
                    features(b, 3)
                if ffn:
                    low(f, 0, 6)
                    low(f, 0, 7)
                    low(f, 1, 0)
                prepare()
                for c in range(C):
                    last = c == C - 1
                    if att:
                        mask_scores(b, c, 0)
                        if c > 0:
                            normalise1(b, c - 1)
                        mask_scores(b, c, 1)
                        if c > 0:
                            low_x1(b, c - 1)
                    if ffn:
                        low(f, 1, 1 + 2 * c)
                    if att:
                        mask_scores(b, c, 2)
                        mask_scores(b, c, 3)
                        invert(b, c)
                    if ffn and last:
                        norm2(f, 0)
                    if att:
                        divide(b, c)
                        if not last:
                            keep_state(b, c)
                    if ffn and last:
                        norm2(f, 1)
                        normalise2(f, 0)
                    if ffn and not last:
                        low(f, 1, 2 + 2 * c)
                    if att:
                        norm1(b, c)
                if ffn:
                    normalise2(f, 1)
                    norm2(f, 2)
                if att:
                    normalise1(b, C - 1)
                if ffn:
                    norm2(f, 3)
                    normalise2(f, 2)
                if att:
                    low_x1(b, C - 1)
                if ffn:
                    normalise2(f, 3)

            def first_weights():
                dve.wait_ge(k0_in, 16)
                for g in range(G):
                    dve.tensor_tensor(w0[:, g, :], k0_raw[:, g, :], k0_raw[:, G + g, :],
                                      ALU.subtract).then_inc(scal, 1)
                dve.wait_ge(scal, 10)
                for g in range(G):
                    dve.tensor_scalar(w0[:, g, :], w0[:, g, :], c0[:], None, ALU.mult).then_inc(w0_ready, 1)

            dve.sem_inc(s_done.sem, 2)
            dve.memset(phi_eps[:], PHI_EPS).then_inc(scal, 1)
            dve.memset(vpad[:], 0.0).then_inc(zeroed, 1)
            dve.wait_ge(const_in, CONST_IN)
            dve.tensor_scalar(s_neg[:], s_raw[:], 0.0, None, ALU.is_lt).then_inc(scal, 1)
            dve.wait_ge(scal, 2)
            dve.scalar_tensor_tensor(out=s_sign[:], in0=s_raw[:], scalar=0.0, in1=s_neg[:], op0=ALU.is_gt,
                                     op1=ALU.subtract).then_inc(scal, 1)
            dve.wait_ge(scal, 3)
            dve.tensor_tensor(s_abs[:], s_raw[:], s_sign[:], ALU.mult).then_inc(scal, 1)
            dve.tensor_scalar(c1[:, 0:1], s_sign[:, 1:2], 2 * H2_SCALE / H1_SCALE, None,
                              ALU.mult).then_inc(scal, 1)
            dve.tensor_scalar(c1[:, 1:2], s_sign[:, 1:2], -H2_SCALE / H1_SCALE, None,
                              ALU.mult).then_inc(scal, 1)
            dve.tensor_scalar(c0[:], s_sign[:, 0:1], 2 * H1_SCALE / X_SCALE, None, ALU.mult).then_inc(scal, 1)
            dve.tensor_copy(ident16[:], ident[:]).then_inc(scal, 1)
            dve.wait_ge(scal, 4)
            dve.tensor_scalar(out_scale[:, 0:1], s_abs[:, 0:1], s_abs[:, 1:2], 4.0 / H2_SCALE, ALU.mult,
                              ALU.mult).then_inc(w0_ready, 1)
            dve.wait_ge(w0_ready, 1)
            dve.tensor_scalar(out_scale[:, 1:2], out_scale[:, 0:1], s_raw[:, 2:3], None,
                              ALU.mult).then_inc(w0_ready, 1)
            step(0, None, first_weights)
            with dve.Fori(0, B - 1) as f:
                step(f + 1, f)
            step(None, B - 1)

        @block.gpsimd
        def _(pool):
            def split_q(b, g):
                pool.wait_ge(feat.sem, feat.at(b, 3 + g))
                for par in range(2):
                    op = pool.tensor_tensor(q_par[:, par, g, :], qf[:, g, :],
                                            parity[:, par:par + 1].to_broadcast([P, T]), ALU.mult)
                op.then_inc(q_split.sem, 1)

            def times_prefix(b, g):
                pool.wait_ge(scanned.sem, scanned.at(b, g + 1))
                pool.tensor_tensor(qz[:, g, :], qf[:, g, :], zc[:, g, :], ALU.mult).then_inc(qz_ready.sem, 1)

            def inverse_std(b, c, mv, rs, step_, stat):
                pool.wait_ge(step_.sem, step_.at(b, 2 * c + 2))
                pool.tensor_tensor(rs[:, c, 0:1], mv[:, c, 1:2], consts[:, 0:1], ALU.add).then_inc(stat.sem, 1)
                pool.wait_ge(stat.sem, stat.at(b, 2 * c + 1))
                pool.tensor_tensor(rs[:, c, 1:2], rs[:, c, 0:1], consts[:, 1:2], ALU.pow).then_inc(stat.sem, 1)

            def step(b, f):
                att, ffn = b is not None, f is not None
                if att:
                    split_q(b, 0)
                    times_prefix(b, 0)
                    split_q(b, 1)
                    times_prefix(b, 1)
                    for c in range(C - 1):
                        inverse_std(b, c, mv1, rs1, ln1_step, ln1_stat)
                if ffn:
                    inverse_std(f, 0, mv2, rs2, ln2_step, ln2_stat)
                    inverse_std(f, 1, mv2, rs2, ln2_step, ln2_stat)
                if att:
                    inverse_std(b, C - 1, mv1, rs1, ln1_step, ln1_stat)
                if ffn:
                    inverse_std(f, 2, mv2, rs2, ln2_step, ln2_stat)
                    inverse_std(f, 3, mv2, rs2, ln2_step, ln2_stat)

            pool.memset(consts[:, 0:1], LN_EPS)
            pool.memset(consts[:, 1:2], -0.5).then_inc(lnc_ready, 1)
            pool.wait_ge(lnc_ready, 1)
            pool.wait_ge(const_in, CONST_IN)
            step(0, None)
            with pool.Fori(0, B - 1) as f:
                step(f + 1, f)
            step(None, B - 1)


def kernel(L0_attn_x, L0_attn_Wq, L0_attn_Wk, L0_attn_Wv, L0_attn_Wo, L0_ffn_k0, L0_ffn_k1, L0_ffn_k2,
           L0_ffn_s0, L0_ffn_s1, L0_ffn_s2):
    import concourse.bacc as bacc
    from concourse.bass_utils import run_bass_kernel_spmd

    x = np.ascontiguousarray(L0_attn_x)
    p = np.arange(P)
    arrays = {
        "x": x,
        "x_t": np.ascontiguousarray(np.transpose(x, (0, 2, 1))),
        "wq_t": np.ascontiguousarray(np.transpose(L0_attn_Wq)),
        "wk_t": np.ascontiguousarray(np.transpose(L0_attn_Wk)),
        "wv_t": np.ascontiguousarray(np.transpose(L0_attn_Wv)),
        "wo_t": np.ascontiguousarray(np.transpose(L0_attn_Wo)),
        "k0": np.ascontiguousarray(L0_ffn_k0),
        "k1": np.ascontiguousarray(L0_ffn_k1),
        "k2": np.ascontiguousarray(L0_ffn_k2),
        "s": np.ascontiguousarray(np.broadcast_to(
            np.stack([np.asarray(L0_ffn_s0), np.asarray(L0_ffn_s1), np.asarray(L0_ffn_s2)])[None, :], (P, 3))),
        "causal": (p[:, None] <= p[None, :]).astype(np.float32),
        "blocks": (p[:, None] // DH == p[None, :] // DH).astype(np.float32),
        "parity": (p[:, None] // DH % 2 == np.arange(2)[None, :]).astype(np.float32),
        "ident": np.eye(P, dtype=np.float32),
    }
    nc = bacc.Bacc("TRN2", target_bir_lowering=False, num_devices=1)
    ins = [nc.dram_tensor(f"{n}_dram", a.shape, mybir.dt.from_np(a.dtype), kind="ExternalInput").ap()
           for n, a in arrays.items()]
    out = nc.dram_tensor("out_dram", (B, T, D), F32, kind="ExternalOutput").ap()
    layer_kernel(nc, *ins, out)
    r = run_bass_kernel_spmd(nc, [{f"{n}_dram": a for n, a in arrays.items()}], core_ids=[0])
    return r.results[0]["out_dram"]
```

```python
from contextlib import ExitStack

import numpy as np

import concourse.bass as bass
from concourse import mybir
from concourse.alu_op_type import AluOpType as ALU

ACT = mybir.ActivationFunctionType
F32 = mybir.dt.float32
F16 = mybir.dt.float16
F32R = mybir.dt.float32r
U8 = mybir.dt.uint8

P = 128
B, T, D = 16, 512, 256
H = 16
DH = D // H
C = T // P
G = D // P
PAIRS = P // (2 * DH)
F = 1024
FT = F // P
PHI_EPS = 1e-6
LN_EPS = 1e-5
CLAMP = 18.0
X_SCALE = 2.0 ** 11
H1_SCALE = 2.0 ** 6
H2_SCALE = 2.0 ** -4
ATT_JOBS = 14
COMBOS = 4
STACK_IN = 16 * PAIRS * COMBOS
FFN_JOBS = 22
CONST_IN = 5 * 16


class Tally:

    def __init__(self, sem, per_sequence):
        self.sem, self.per = sem, per_sequence

    def at(self, b, n):
        return b * self.per + n


def layer_kernel(nc, x, x_t, wq_t, wk_t, wv_t, wo_t, k0, k1, k2, s_in, causal_in, blocks_in, ident_in, parity_in, out):
    x_rows = x.rearrange("b (c p) d -> b p c d", p=P)
    out_rows = out.rearrange("b (c p) d -> b p c d", p=P)
    xt_rows = x_t.rearrange("b (g p) t -> b p g t", p=P)

    ctx = ExitStack()
    with ctx:
        def sb(name, shape, dt=F32):
            return ctx.enter_context(nc.sbuf_tensor(name, shape, dt))

        def sem(name):
            return ctx.enter_context(nc.semaphore(name))

        def tally(name, per):
            return Tally(sem(name), per)

        wq, wk, wv, wo = (sb(n, [P, G, D]) for n in ("wq", "wk", "wv", "wo"))
        causal = sb("causal", [P, P])
        blocks = sb("blocks", [P, P])
        blocks_r = sb("blocks_r", [P, P], F32R)
        ident = sb("ident", [P, P])
        parity = sb("parity", [P, 2])
        ident16 = sb("ident16", [P, P], F16)
        w0 = sb("w0", [P, G, F], F16)
        w1 = sb("w1", [P, FT, F], F16)
        w2 = sb("w2", [P, FT, D], F16)
        s_raw = sb("s_raw", [P, 3])
        s_neg = sb("s_neg", [P, 3])
        s_sign = sb("s_sign", [P, 3])
        s_abs = sb("s_abs", [P, 3])
        c0 = sb("c0", [P, 1])
        c1 = sb("c1", [P, 2])
        out_scale = sb("out_scale", [P, 2])
        phi_eps = sb("phi_eps", [P, 1])
        consts = sb("consts", [P, 3])
        xt_sb = sb("xt_sb", [P, G, T])
        x_sb = sb("x_sb", [P, C, D])
        soft_at = nc.sbuf_base
        soft = sb("soft", [P, 2, T])
        qf = sb("qf", [P, G, T])
        kf = sb("kf", [P, G, T])
        k_parts = sb("k_parts", [P, 2, G, T], F32R)
        q_parts = sb("q_parts", [P, 2, G, 2, T], F32R)
        k_stack = sb("k_stack", [P, PAIRS, G, T], F32R)
        q_stack = sb("q_stack", [P, PAIRS, G, 2, T], F32R)
        zc_at = nc.sbuf_base
        zc = sb("zc", [P, G, T])
        vpad = sb("vpad", [P, C, H // 2, 4 * DH])
        z_high = nc.alloc_sbuf_tensor_at("z_high", [P, G, T], F32R, offset=soft_at)
        z_low = nc.alloc_sbuf_tensor_at("z_low", [P, G, T], F32R, offset=zc_at)
        k_tok = sb("k_tok", [P, C - 1, D])
        s_sb = sb("s_sb", [P, 4, 4, P])
        kv_sb = sb("kv_sb", [P, G, P])
        den = sb("den", [P, G, T])
        attn = sb("attn", [P, G, P])
        st1 = sb("st1", [P, 7])
        mv1 = sb("mv1", [P, C, 2])
        rs1 = sb("rs1", [P, C, 2])
        x1 = sb("x1", [P, C, D])
        x1h = sb("x1h", [P, C, D], F16)
        x1l = sb("x1l", [P, C, D], F16)
        x1_keep = sb("x1_keep", [P, C, D])
        x1t = sb("x1t", [P, 2, G, T], F16)
        h1 = sb("h1", [P, 2, FT, T], F16)
        h2 = sb("h2", [P, 2, FT, T], F16)
        raw = h2[:].bitcast(U8).rearrange("p h m t -> p (h m t)")
        k0_raw = raw[:, 0:2 * G * F].rearrange("p (g n) -> p g n", n=F)
        k1_raw = raw[:, 2 * G * F:(2 * G + FT) * F].rearrange("p (g n) -> p g n", n=F)
        k2_raw = raw[:, (2 * G + FT) * F:(2 * G + FT) * F + FT * D].rearrange("p (g n) -> p g n", n=D)
        y = sb("y", [P, C, D])
        st2 = sb("st2", [P, 7])
        mv2 = sb("mv2", [P, C, 2])
        rs2 = sb("rs2", [P, C, 4])

        def bank(name):
            return ctx.enter_context(nc.psum_tensor(name, [P, 512], F32))

        ffn_ps = [bank("ffn_ps0"), bank("ffn_ps1")]
        att_ps = [bank("att_ps0"), bank("att_ps1")]
        s_ps = [bank("s_ps0"), bank("s_ps1")]
        h1_ps = ffn_ps + s_ps
        num_ps = bank("num_ps")
        kv_ps = bank("kv_ps")
        num_v = num_ps[:, 0:G * P].rearrange("p (g t) -> p g t", g=G)
        kv_v = kv_ps[:, 0:G * P].rearrange("p (g t) -> p g t", g=G)

        wk_in, wq_in, wv_in, wo_in = sem("wk_in"), sem("wq_in"), sem("wv_in"), sem("wo_in")
        const_in, k0_in, k1_in, k2_in = sem("const_in"), sem("k0_in"), sem("k1_in"), sem("k2_in")
        scal = sem("scal")
        lnc_ready = sem("lnc_ready")
        zeroed = sem("zeroed")
        blocks_ready = sem("blocks_ready")
        w0_ready, w12_ready = sem("w0_ready"), sem("w12_ready")
        xt_in = tally("xt_in", 16)
        x_in = [tally(f"x_in{c}", 16) for c in range(C)]
        y_out = [tally(f"y_out{c}", 16) for c in range(C)]
        att_full = tally("att_full", ATT_JOBS)
        clamped = tally("clamped", 4)
        exped = tally("exped", 4)
        logged = tally("logged", 4)
        feat = tally("feat", 4)
        scanned = tally("scanned", G)
        k_high = tally("k_high", G)
        k_low = tally("k_low", G)
        q_high = tally("q_high", 2 * G)
        q_low = tally("q_low", 2 * G)
        k_stacked = tally("k_stacked", STACK_IN)
        q_stacked = tally("q_stacked", STACK_IN)
        q_half_in = sem("q_half_in")
        qz_ready = tally("qz_ready", G)
        z_high_ready = tally("z_high_ready", G)
        z_low_ready = tally("z_low_ready", G)
        v_ready = tally("v_ready", C)
        kt_ready = tally("kt_ready", C - 1)
        s_full = tally("s_full", 4 * C)
        s_done = tally("s_done", 4 * C)
        num_full = tally("num_full", C)
        kv_full = tally("kv_full", C - 1)
        kv_ready = tally("kv_ready", C - 1)
        den_ready = tally("den_ready", G)
        rden_ready = tally("rden_ready", C)
        attn_ready = tally("attn_ready", C)
        ln1_sum = tally("ln1_sum", C)
        ln1_step = tally("ln1_step", 2 * C)
        ln1_stat = tally("ln1_stat", 2 * C)
        x1_ready = tally("x1_ready", C)
        x1h_ready = tally("x1h_ready", C)
        x1l_ready = tally("x1l_ready", C)
        ffn_full = tally("ffn_full", FFN_JOBS)
        x1_kept = tally("x1_kept", 1)
        x1t_ready = [tally(f"x1t_ready{i}", 1) for i in range(2)]
        high_ready = tally("high_ready", 2 * FT)
        low_ready = tally("low_ready", 2 * FT)
        ln2_sum = tally("ln2_sum", C)
        ln2_step = tally("ln2_step", 2 * C)
        ln2_stat = tally("ln2_stat", 4 * C)
        y_ready = tally("y_ready", C)

        block = ctx.enter_context(nc.Block())

        @block.sync
        def _(sp):
            def load_x(b):
                sp.dma_start(xt_sb[:], xt_rows[b]).then_inc(xt_in.sem, 16)

            def stack_k(b):
                for i in (0, 2, 1, 3):
                    if i % 2 == 0:
                        sp.wait_ge(k_high.sem, k_high.at(b, G))
                    else:
                        sp.wait_ge(k_low.sem, k_low.at(b, G))
                    for a in range(PAIRS):
                        sp.dma_start(k_stack[2 * DH * i:2 * DH * (i + 1), a].bitcast(F32),
                                     k_parts[2 * DH * a:2 * DH * (a + 1), i % 2].bitcast(F32)
                                     ).then_inc(k_stacked.sem, 16)

            def stack_q(b, tokens, done):
                for i in range(COMBOS):
                    if i // 2 == 0:
                        sp.wait_ge(q_high.sem, q_high.at(b, 2 * G))
                    else:
                        sp.wait_ge(q_low.sem, q_low.at(b, 2 * G))
                    for a in range(PAIRS):
                        sp.dma_start(q_stack[2 * DH * i:2 * DH * (i + 1), a, :, :, tokens].bitcast(F32),
                                     q_parts[2 * DH * a:2 * DH * (a + 1), i // 2, :, :, tokens].bitcast(F32)
                                     ).then_inc(done, 16)

            def load_rows(b, c):
                sp.dma_start(x_sb[:, c, :], x_rows[b, :, c, :]).then_inc(x_in[c].sem, 16)

            def reload(b):
                sp.wait_ge(att_full.sem, att_full.at(b - 1, 6))
                load_x(b)
                for c in range(C):
                    sp.wait_ge(ln1_sum.sem, ln1_sum.at(b - 1, c + 1))
                    load_rows(b, c)

            def store(f):
                for c in range(C):
                    sp.wait_ge(y_ready.sem, y_ready.at(f, c + 1))
                    sp.dma_start(out_rows[f, :, c, :], y[:, c, :]).then_inc(y_out[c].sem, 16)

            sp.dma_start(wk[:], wk_t.rearrange("(g p) n -> p g n", p=P)).then_inc(wk_in, 16)
            load_x(0)
            sp.dma_start(wq[:], wq_t.rearrange("(g p) n -> p g n", p=P)).then_inc(wq_in, 16)
            sp.dma_start(causal[:], causal_in).then_inc(const_in, 16)
            sp.dma_start(blocks[:], blocks_in).then_inc(const_in, 16)
            sp.dma_start(ident[:], ident_in).then_inc(const_in, 16)
            sp.dma_start(parity[:], parity_in).then_inc(const_in, 16)
            sp.dma_start(s_raw[:], s_in).then_inc(const_in, 16)
            sp.dma_start(wv[:], wv_t.rearrange("(g p) n -> p g n", p=P)).then_inc(wv_in, 16)
            sp.dma_start(wo[:], wo_t.rearrange("(g p) n -> p g n", p=P)).then_inc(wo_in, 16)
            for c in range(C):
                load_rows(0, c)
            sp.dma_start(k0_raw, k0.rearrange("(g p) n -> p g n", p=P)).then_inc(k0_in, 16)
            sp.dma_start(k1_raw, k1.rearrange("(g p) n -> p g n", p=P)).then_inc(k1_in, 16)
            sp.dma_start(k2_raw, k2.rearrange("(g p) n -> p g n", p=P)).then_inc(k2_in, 16)
            stack_k(0)
            stack_q(0, slice(0, T // 2), q_half_in)
            stack_q(0, slice(T // 2, T), q_stacked.sem)
            reload(1)
            with sp.Fori(0, B - 2) as f:
                stack_k(f + 1)
                stack_q(f + 1, slice(0, T), q_stacked.sem)
                reload(f + 2)
                store(f)
            stack_k(B - 1)
            stack_q(B - 1, slice(0, T), q_stacked.sem)
            store(B - 2)
            store(B - 1)
            for c in range(C):
                sp.wait_ge(y_out[c].sem, y_out[c].at(B, 16))

        @block.tensor
        def _(pe):
            def att_bank(b, n, first=False):
                if n >= 12:
                    pe.wait_ge(ln1_sum.sem, ln1_sum.at(b, n - 11))
                elif n >= 10:
                    pe.wait_ge(kt_ready.sem, kt_ready.at(b, n - 8))
                elif n >= 8:
                    pe.wait_ge(den_ready.sem, den_ready.at(b, n - 7))
                elif n >= 6:
                    pe.wait_ge(v_ready.sem, v_ready.at(b, 2 * (n - 5)))
                elif n >= 2:
                    pe.wait_ge(feat.sem, feat.at(b, n - 1))
                elif not first:
                    pe.wait_ge(ln1_sum.sem, ln1_sum.at(b - 1, C - 1 + n))
                return att_ps[n % 2]

            def hidden1_bank(f, m):
                if m < 2:
                    pe.wait_ge(ln2_sum.sem, ln2_sum.at(f, C - 1 + m))
                elif m < 4:
                    pe.wait_ge(x1t_ready[m - 2].sem, x1t_ready[m - 2].at(f, 1))
                else:
                    pe.wait_ge(low_ready.sem, low_ready.at(f, m - 3))
                return h1_ps[m % 4]

            def ffn_bank(f, n):
                if n >= 4 + 2 * FT:
                    pe.wait_ge(ln2_sum.sem, ln2_sum.at(f, C + n - 3 - 2 * FT))
                elif n >= 4 + FT:
                    pe.wait_ge(low_ready.sem, low_ready.at(f, n - 3))
                else:
                    pe.wait_ge(low_ready.sem, low_ready.at(f, n - 5))
                return ffn_ps[n % 2]

            def project(b, n, w, g, first=False):
                ps = att_bank(b, n, first)
                for d in range(G):
                    mm = pe.matmul(ps[:], w[:, d, g * P:(g + 1) * P], xt_sb[:, d, :],
                                   start=(d == 0), stop=(d == G - 1))
                mm.then_inc(att_full.sem, 1)

            def project_v(b, half):
                ps = att_bank(b, 4 + half)
                for i in range(2):
                    c = 2 * half + i
                    for d in range(G):
                        mm = pe.matmul(ps[:, i * D:(i + 1) * D], xt_sb[:, d, c * P:(c + 1) * P], wv[:, d, :],
                                       start=(d == 0), stop=(d == G - 1))
                mm.then_inc(att_full.sem, 1)

            def transpose_k(b, n, chunks):
                ps = att_bank(b, n)
                pe.wait_ge(const_in, CONST_IN)
                pe.wait_ge(feat.sem, feat.at(b, 2))
                for i, c in enumerate(chunks):
                    for g in range(G):
                        mm = pe.transpose(ps[:, i * D + g * P:i * D + (g + 1) * P],
                                          kf[:, g, c * P:(c + 1) * P], ident[:])
                mm.then_inc(att_full.sem, 1)

            def scores(b, f, c, job):
                n = c * 4 + job
                if n >= 2:
                    pe.wait_ge(s_done.sem, s_done.at(b, n + 1))
                elif f is not None:
                    pe.wait_ge(low_ready.sem, low_ready.at(f, FT - 1 + n))
                g = job // 2
                pe.wait_ge(k_stacked.sem, k_stacked.at(b, STACK_IN))
                if f is None and c < C // 2:
                    pe.wait_ge(q_half_in, STACK_IN)
                else:
                    pe.wait_ge(q_stacked.sem, q_stacked.at(b, STACK_IN))
                for i in range(2):
                    a = 2 * (job % 2) + i
                    mm = pe.matmul(s_ps[job % 2][:, i * 2 * P:(i + 1) * 2 * P],
                                   k_stack[:, a, g, c * P:(c + 1) * P],
                                   q_stack[:, a, g, :, c * P:(c + 1) * P], start=True, stop=True)
                mm.then_inc(s_full.sem, 1)

            def denominator(b, n, g):
                ps = att_bank(b, n)
                pe.wait_ge(blocks_ready, 1)
                pe.wait_ge(z_low_ready.sem, z_low_ready.at(b, g + 1))
                pe.matmul(ps[:], blocks_r[:], z_high[:, g, :], start=True, stop=False)
                pe.matmul(ps[:], blocks_r[:], z_low[:, g, :], start=False, stop=True).then_inc(att_full.sem, 1)

            def weigh(b, c):
                if c > 0:
                    pe.wait_ge(kv_ready.sem, kv_ready.at(b, c))
                    for g in range(G):
                        pe.matmul(num_v[:, g, :], kv_sb[:, g, :], qf[:, g, c * P:(c + 1) * P],
                                  start=(g == 0), stop=False, skip_group_check=True)
                pe.wait_ge(v_ready.sem, v_ready.at(b, c + 1))
                for g in range(G):
                    pe.wait_ge(s_done.sem, s_done.at(b, 4 * c + 2 * (g + 1) + 2))
                    for par in range(2):
                        for a in range(PAIRS):
                            pair = g * PAIRS + a
                            mm = pe.matmul(num_v[2 * DH * a:2 * DH * (a + 1), g, :],
                                           vpad[:, c, pair, par * 2 * DH:(par + 1) * 2 * DH],
                                           s_sb[:, 2 * g + a // 2, 2 * (a % 2) + par, :],
                                           start=(c == 0 and g == 0 and par == 0), stop=(par == 1),
                                           skip_group_check=True)
                mm.then_inc(num_full.sem, 1)
                if c < C - 1:
                    pe.wait_ge(kt_ready.sem, kt_ready.at(b, c + 1))
                    for g in range(G):
                        v = vpad[:, c, g * PAIRS:(g + 1) * PAIRS, :].rearrange(
                            "p a (q e) -> p a q e", e=DH)[:, :, 0:4:3, :]
                        mm = pe.matmul(kv_v[:, g, :], k_tok[:, c, g * P:(g + 1) * P], v,
                                       start=(c == 0 and g == 0), stop=True, skip_group_check=True)
                    mm.then_inc(kv_full.sem, 1)

            def project_out(b, c):
                ps = att_bank(b, 10 + c)
                pe.wait_ge(attn_ready.sem, attn_ready.at(b, c + 1))
                for g in range(G):
                    mm = pe.matmul(ps[:, 0:D], attn[:, g, :], wo[:, g, :],
                                   start=(g == 0), stop=(g == G - 1))
                mm.then_inc(att_full.sem, 1)

            def transpose_x1(f, half):
                pe.wait_ge(s_done.sem, s_done.at(f, 4 * C + 2))
                ps = s_ps[half][:].bitcast(F16).rearrange("p (c h g t) -> p c h g t", c=2, h=2, g=G)
                pe.wait_ge(x1l_ready.sem, x1l_ready.at(f, 2 * half + 2))
                for i in range(2):
                    for h, part in enumerate((x1h, x1l)):
                        for g in range(G):
                            mm = pe.transpose(ps[:, i, h, g, :],
                                              part[:, 2 * half + i, g * P:(g + 1) * P], ident16[:])
                mm.then_inc(ffn_full.sem, 1)

            def hidden1(f, m):
                ps = hidden1_bank(f, m)
                if m == 0:
                    pe.wait_ge(x1t_ready[0].sem, x1t_ready[0].at(f, 1))
                    pe.wait_ge(x1t_ready[1].sem, x1t_ready[1].at(f, 1))
                for d in range(G):
                    for h in range(2):
                        mm = pe.matmul(ps[:], w0[:, d, m * P:(m + 1) * P], x1t[:, h, d, :],
                                       start=(d == 0 and h == 0), stop=(d == G - 1 and h == 1))
                mm.then_inc(ffn_full.sem, 1)

            def hidden2(f, m, start=0, stop=FT):
                ps = ffn_ps[m % 2]
                if start == 0:
                    ffn_bank(f, 2 + FT + m)
                for d in range(start, stop):
                    if m == 0:
                        pe.wait_ge(low_ready.sem, low_ready.at(f, d + 1))
                    for h in range(2):
                        mm = pe.matmul(ps[:], w1[:, d, m * P:(m + 1) * P], h1[:, h, d, :],
                                       start=(d == 0 and h == 0), stop=(d == FT - 1 and h == 1))
                if stop == FT:
                    mm.then_inc(ffn_full.sem, 1)

            def ffn_out(f, c, start=0, stop=FT):
                ps = ffn_ps[c % 2]
                if start == 0:
                    ffn_bank(f, 2 + 2 * FT + c)
                for d in range(start, stop):
                    if c == 0:
                        pe.wait_ge(low_ready.sem, low_ready.at(f, FT + d + 1))
                    for h in range(2):
                        mm = pe.matmul(ps[:, 0:D], h2[:, h, d, c * P:(c + 1) * P], w2[:, d, :],
                                       start=(d == 0 and h == 0), stop=(d == FT - 1 and h == 1))
                if stop == FT:
                    mm.then_inc(ffn_full.sem, 1)

            def fill(f, c, part):
                if c < C - 1:
                    hidden2(f, 5 + c, 3 * part, min(3 * part + 3, FT))
                elif part < 2:
                    ffn_out(f, part)
                else:
                    ffn_out(f, 2, 0, FT // 2)

            def step(b, f):
                att, ffn = b is not None, f is not None
                if ffn:
                    transpose_x1(f, 0)
                if att:
                    pe.wait_ge(xt_in.sem, xt_in.at(b, 16))
                    project(b, 0, wk, 0, not ffn)
                if ffn:
                    transpose_x1(f, 1)
                if att:
                    project(b, 1, wk, 1, not ffn)
                if ffn:
                    hidden1(f, 0)
                    hidden1(f, 1)
                if att:
                    if not ffn:
                        pe.wait_ge(wq_in, 16)
                    project(b, 2, wq, 0)
                if ffn:
                    hidden1(f, 2)
                if att:
                    project(b, 3, wq, 1)
                if ffn:
                    hidden1(f, 3)
                    hidden1(f, 4)
                    hidden1(f, 5)
                if att:
                    if not ffn:
                        pe.wait_ge(wv_in, 16)
                    project_v(b, 0)
                if ffn:
                    hidden1(f, 6)
                    hidden1(f, 7)
                if att:
                    project_v(b, 1)
                if ffn:
                    hidden2(f, 0)
                if att:
                    denominator(b, 6, 0)
                    denominator(b, 7, 1)
                if ffn:
                    hidden2(f, 1)
                if att:
                    transpose_k(b, 8, (0, 1))
                    transpose_k(b, 9, (2,))
                if ffn:
                    hidden2(f, 2)
                    hidden2(f, 3)
                    hidden2(f, 4)
                if att and not ffn:
                    pe.wait_ge(zeroed, 1)
                    pe.wait_ge(wo_in, 16)
                if att:
                    scores(b, f, 0, 0)
                    scores(b, f, 0, 1)
                for c in range(C):
                    if ffn:
                        fill(f, c, 0)
                    if att and (ffn or c == 0):
                        scores(b, f, c, 2)
                        scores(b, f, c, 3)
                    if ffn:
                        fill(f, c, 1)
                    if att:
                        weigh(b, c)
                        if c < C - 1:
                            scores(b, f, c + 1, 0)
                            scores(b, f, c + 1, 1)
                            if not ffn:
                                scores(b, f, c + 1, 2)
                                scores(b, f, c + 1, 3)
                    if ffn:
                        fill(f, c, 2)
                    if att:
                        project_out(b, c)
                if ffn:
                    ffn_out(f, 2, FT // 2)
                    ffn_out(f, 3)

            pe.wait_ge(wk_in, 16)
            step(0, None)
            pe.wait_ge(scal, 8)
            pe.wait_ge(w0_ready, 2 + G)
            pe.wait_ge(w12_ready, 2 * FT)
            with pe.Fori(0, B - 1) as f:
                step(f + 1, f)
            step(None, B - 1)

        @block.scalar
        def _(act):
            def exp(b, n):
                s = soft[:, n % 2, :]
                act.wait_ge(clamped.sem, clamped.at(b, n + 1))
                act.activation(s, s, ACT.Exp).then_inc(exped.sem, 1)

            def log(b, n):
                s = soft[:, n % 2, :]
                act.wait_ge(exped.sem, exped.at(b, n + 1))
                act.activation(s, s, ACT.Ln, bias=1.0).then_inc(logged.sem, 1)

            def high_features(b, n):
                act.wait_ge(feat.sem, feat.at(b, n + 1))
                g = n % 2
                if n < G:
                    act.activation(k_parts[:, 0, g, :], kf[:, g, :], ACT.Copy).then_inc(k_high.sem, 1)
                    return
                for par in range(2):
                    act.activation(q_parts[:, 0, g, par, :], qf[:, g, :], ACT.Identity,
                                   scale=parity[:, par:par + 1]).then_inc(q_high.sem, 1)

            def pad_v(b, half):
                act.wait_ge(att_full.sem, att_full.at(b, 4 + half + 1))
                for i in range(2):
                    c = 2 * half + i
                    to = vpad[:, c, :, :].rearrange("p a (q e) -> p a q e", e=DH)[:, :, 0:4:3, :]
                    of = att_ps[half][:, i * D:(i + 1) * D].rearrange("p (a q e) -> p a q e", q=2, e=DH)
                    act.activation(to, of, ACT.Copy).then_inc(v_ready.sem, 1)

            def keep_k(b, n, chunks):
                act.wait_ge(att_full.sem, att_full.at(b, n + 1))
                for i, c in enumerate(chunks):
                    act.activation(k_tok[:, c, :], att_ps[n % 2][:, i * D:(i + 1) * D],
                                   ACT.Copy).then_inc(kt_ready.sem, 1)

            def denominator(b, g):
                act.wait_ge(att_full.sem, att_full.at(b, 7 + g))
                act.activation(den[:, g, :], att_ps[g][:], ACT.Identity, bias=phi_eps[:]).then_inc(den_ready.sem, 1)

            def high_z(b, g):
                act.wait_ge(qz_ready.sem, qz_ready.at(b, g + 1))
                act.activation(z_high[:, g, :], zc[:, g, :], ACT.Copy).then_inc(z_high_ready.sem, 1)

            def high_x1(b, c):
                act.wait_ge(x1_ready.sem, x1_ready.at(b, c + 1))
                act.activation(x1h[:, c, :], x1[:, c, :], ACT.Copy, scale=X_SCALE).then_inc(x1h_ready.sem, 1)

            def normalise2(f, c):
                act.wait_ge(ln2_stat.sem, ln2_stat.at(f, 4 * c + 4))
                act.activation(y[:, c, :], y[:, c, :], ACT.Identity, scale=rs2[:, c, 1:2],
                               bias=rs2[:, c, 3:4]).then_inc(y_ready.sem, 1)

            def keep_x1(f):
                act.wait_ge(x1_ready.sem, x1_ready.at(f, C))
                act.wait_ge(ln2_sum.sem, ln2_sum.at(f, C))
                act.activation(x1_keep[:], x1[:], ACT.Copy).then_inc(x1_kept.sem, 1)

            def high(f, layer, m):
                n = layer * FT + m
                act.wait_ge(ffn_full.sem, ffn_full.at(f, 2 + n + 1))
                to, of = ((h1, h1_ps[m % 4]), (h2, ffn_ps[m % 2]))[layer]
                act.activation(to[:, 0, m, :], of[:], ACT.Relu).then_inc(high_ready.sem, 1)

            def step(b, f, prepare=lambda: None):
                att, ffn = b is not None, f is not None
                if att:
                    exp(b, 0)
                    log(b, 0)
                    exp(b, 1)
                    log(b, 1)
                if ffn:
                    high(f, 0, 0)
                if att:
                    high_features(b, 0)
                if ffn:
                    high(f, 0, 1)
                if att:
                    high_features(b, 1)
                    exp(b, 2)
                    log(b, 2)
                if ffn:
                    high(f, 0, 2)
                if att:
                    exp(b, 3)
                    log(b, 3)
                if ffn:
                    high(f, 0, 3)
                if att:
                    high_z(b, 0)
                    high_features(b, 2)
                if ffn:
                    high(f, 0, 4)
                    high(f, 0, 5)
                if att:
                    high_features(b, 3)
                    pad_v(b, 0)
                if ffn:
                    high(f, 0, 6)
                    high(f, 0, 7)
                if att:
                    high_z(b, 1)
                    pad_v(b, 1)
                if ffn:
                    keep_x1(f)
                    high(f, 1, 0)
                if att:
                    denominator(b, 0)
                    denominator(b, 1)
                if ffn:
                    high(f, 1, 1)
                if att:
                    keep_k(b, 8, (0, 1))
                    keep_k(b, 9, (2,))
                if ffn:
                    high(f, 1, 2)
                    high(f, 1, 3)
                    high(f, 1, 4)
                prepare()
                for c in range(C):
                    if att and c > 0:
                        high_x1(b, c - 1)
                    if ffn and c < C - 1:
                        high(f, 1, 5 + c)
                if ffn:
                    normalise2(f, 0)
                    normalise2(f, 1)
                if att:
                    high_x1(b, C - 1)
                if ffn:
                    normalise2(f, 2)
                    normalise2(f, 3)

            def signs():
                act.wait_ge(scal, 6)
                act.wait_ge(k1_in, 16)
                act.wait_ge(k2_in, 16)
                for d in range(FT):
                    act.activation(w1[:, d, :], k1_raw[:, d, :], ACT.Identity, bias=c1[:, 1:2],
                                   scale=c1[:, 0:1]).then_inc(w12_ready, 1)
                for d in range(FT):
                    act.activation(w2[:, d, :], k2_raw[:, d, :], ACT.Copy, bias=-1.0,
                                   scale=2.0).then_inc(w12_ready, 1)

            act.sem_inc(x1_kept.sem, 1)
            act.sem_inc(ln2_sum.sem, C)
            for c in range(C):
                act.sem_inc(y_out[c].sem, 16)
            act.preload_act_table_set("natural_log_exp_and_others")
            act.wait_ge(scal, 1)
            step(0, None, signs)
            with act.Fori(0, B - 1) as f:
                step(f + 1, f)
            step(None, B - 1)

        @block.vector
        def _(dve):
            def clamp(b, n):
                dve.wait_ge(att_full.sem, att_full.at(b, n + 1))
                dve.tensor_scalar(soft[:, n % 2, :], att_ps[n % 2][:], CLAMP, None,
                                  ALU.min).then_inc(clamped.sem, 1)

            def features(b, n):
                dve.wait_ge(logged.sem, logged.at(b, n + 1))
                to = (kf, qf)[n // 2][:, n % 2, :]
                dve.scalar_tensor_tensor(out=to, in0=soft[:, n % 2, :], scalar=PHI_EPS,
                                         in1=att_ps[n % 2][:], op0=ALU.add, op1=ALU.max).then_inc(feat.sem, 1)

            def low_q(b, g):
                for par in range(2):
                    dve.wait_ge(q_high.sem, q_high.at(b, 2 * g + par + 1))
                    dve.scalar_tensor_tensor(out=q_parts[:, 1, g, par, :], in0=qf[:, g, :],
                                             scalar=parity[:, par:par + 1],
                                             in1=q_parts[:, 0, g, par, :].bitcast(F32), op0=ALU.mult,
                                             op1=ALU.subtract).then_inc(q_low.sem, 1)

            def prefix(b, g):
                dve.wait_ge(feat.sem, feat.at(b, g + 1))
                dve.tensor_tensor_scan(out=zc[:, g, :], data0=kf[:, g, :], data1=kf[:, g, :], initial=0.0,
                                       op0=ALU.add, op1=ALU.bypass).then_inc(scanned.sem, 1)

            def mask_scores(b, c, job):
                n = c * 4 + job
                dve.wait_ge(s_full.sem, s_full.at(b, n + 1))
                dve.tensor_tensor(s_sb[:, job, :, :], s_ps[job % 2][:].rearrange("p (h t) -> p h t", t=P),
                                  causal[:].unsqueeze(1).to_broadcast([P, 4, P]),
                                  ALU.mult).then_inc(s_done.sem, 1)

            def invert(b, c):
                dve.wait_ge(den_ready.sem, den_ready.at(b, G))
                dve.reciprocal(den[:, :, c * P:(c + 1) * P],
                               den[:, :, c * P:(c + 1) * P]).then_inc(rden_ready.sem, 1)

            def divide(b, c):
                dve.wait_ge(rden_ready.sem, rden_ready.at(b, c + 1))
                dve.wait_ge(num_full.sem, num_full.at(b, c + 1))
                dve.tensor_tensor(attn[:], num_v, den[:, :, c * P:(c + 1) * P], ALU.mult).then_inc(attn_ready.sem, 1)

            def keep_state(b, c):
                dve.wait_ge(kv_full.sem, kv_full.at(b, c + 1))
                dve.tensor_tensor(kv_sb[:], kv_v, blocks[:].unsqueeze(1).to_broadcast([P, G, P]),
                                  ALU.mult).then_inc(kv_ready.sem, 1)

            def statistics(b, c, r, st, mv, step_):
                dve.bn_stats(st[:, 0:6], r[:, c, :]).then_inc(step_.sem, 1)
                dve.wait_ge(step_.sem, step_.at(b, 2 * c + 1))
                dve.tensor_copy(st[:, 6:7], st[:, 0:1])
                dve.bn_aggr(mv[:, c, :], st[:, 0:6]).then_inc(step_.sem, 1)

            def norm1(b, c):
                n = 10 + c
                dve.wait_ge(att_full.sem, att_full.at(b, n + 1))
                dve.wait_ge(x_in[c].sem, x_in[c].at(b, 16))
                dve.wait_ge(x1_kept.sem, x1_kept.at(b, 1))
                dve.tensor_tensor(x1[:, c, :], att_ps[n % 2][:, 0:D], x_sb[:, c, :],
                                  ALU.add).then_inc(ln1_sum.sem, 1)
                dve.wait_ge(ln1_sum.sem, ln1_sum.at(b, c + 1))
                statistics(b, c, x1, st1, mv1, ln1_step)

            def normalise1(b, c):
                dve.wait_ge(ln1_stat.sem, ln1_stat.at(b, 2 * c + 2))
                dve.tensor_scalar(x1[:, c, :], x1[:, c, :], mv1[:, c, 0:1], rs1[:, c, 1:2], ALU.subtract,
                                  ALU.mult).then_inc(x1_ready.sem, 1)

            def low_x1(b, c):
                dve.wait_ge(x1h_ready.sem, x1h_ready.at(b, c + 1))
                dve.scalar_tensor_tensor(out=x1l[:, c, :], in0=x1[:, c, :], scalar=X_SCALE,
                                         in1=x1h[:, c, :], op0=ALU.mult,
                                         op1=ALU.subtract).then_inc(x1l_ready.sem, 1)

            def keep_x1t(f, half):
                dve.wait_ge(ffn_full.sem, ffn_full.at(f, half + 1))
                dve.tensor_copy(x1t[:, :, :, half * 2 * P:(half + 1) * 2 * P].rearrange(
                                    "p h g (c t) -> p c (h g) t", c=2),
                                s_ps[half][:].bitcast(F16).rearrange("p (c h t) -> p c h t", c=2, h=2 * G)
                                ).then_inc(x1t_ready[half].sem, 1)

            def low(f, layer, m):
                n = layer * FT + m
                to, of = ((h1, h1_ps[m % 4]), (h2, ffn_ps[m % 2]))[layer]
                dve.wait_ge(high_ready.sem, high_ready.at(f, n + 1))
                dve.scalar_tensor_tensor(out=to[:, 1, m, :], in0=of[:], scalar=0.0,
                                         in1=to[:, 0, m, :], op0=ALU.max,
                                         op1=ALU.subtract).then_inc(low_ready.sem, 1)

            def norm2(f, c):
                n = c
                dve.wait_ge(ffn_full.sem, ffn_full.at(f, 2 + 2 * FT + c + 1))
                dve.wait_ge(x1_kept.sem, x1_kept.at(f, 2))
                dve.wait_ge(y_out[c].sem, y_out[c].at(f, 16))
                dve.scalar_tensor_tensor(out=y[:, c, :], in0=ffn_ps[n % 2][:, 0:D], scalar=out_scale[:, 1:2],
                                         in1=x1_keep[:, c, :], op0=ALU.mult,
                                         op1=ALU.add).then_inc(ln2_sum.sem, 1)
                dve.wait_ge(ln2_sum.sem, ln2_sum.at(f, C + c + 1))
                statistics(f, c, y, st2, mv2, ln2_step)

            def step(b, f, prepare=lambda: None):
                att, ffn = b is not None, f is not None
                if ffn:
                    keep_x1t(f, 0)
                if att:
                    clamp(b, 0)
                if ffn:
                    keep_x1t(f, 1)
                if att:
                    clamp(b, 1)
                    features(b, 0)
                    prefix(b, 0)
                    features(b, 1)
                if ffn:
                    low(f, 0, 0)
                    low(f, 0, 1)
                if att:
                    clamp(b, 2)
                    prefix(b, 1)
                if ffn:
                    low(f, 0, 2)
                if att:
                    features(b, 2)
                    clamp(b, 3)
                if ffn:
                    low(f, 0, 3)
                if att:
                    features(b, 3)
                    low_q(b, 0)
                if ffn:
                    low(f, 0, 4)
                if att:
                    low_q(b, 1)
                if ffn:
                    low(f, 0, 5)
                    low(f, 0, 6)
                    low(f, 0, 7)
                    low(f, 1, 0)
                prepare()
                if att:
                    invert(b, 0)
                    invert(b, 1)
                if ffn:
                    low(f, 1, 1)
                if att:
                    invert(b, 2)
                if ffn:
                    low(f, 1, 2)
                if att:
                    invert(b, 3)
                if ffn:
                    low(f, 1, 3)
                if att:
                    mask_scores(b, 0, 0)
                    mask_scores(b, 0, 1)
                if ffn:
                    low(f, 1, 4)
                for c in range(C - 1):
                    if att and (ffn or c == 0):
                        mask_scores(b, c, 2)
                        if c > 0:
                            normalise1(b, c - 1)
                        mask_scores(b, c, 3)
                        if c > 0:
                            low_x1(b, c - 1)
                    if att:
                        divide(b, c)
                        keep_state(b, c)
                        mask_scores(b, c + 1, 0)
                        mask_scores(b, c + 1, 1)
                    if att and not ffn:
                        mask_scores(b, c + 1, 2)
                        mask_scores(b, c + 1, 3)
                        if c > 0:
                            normalise1(b, c - 1)
                            low_x1(b, c - 1)
                    if ffn:
                        low(f, 1, 5 + c)
                    if att:
                        norm1(b, c)
                if att and ffn:
                    mask_scores(b, C - 1, 2)
                    mask_scores(b, C - 1, 3)
                if ffn:
                    norm2(f, 0)
                if att and not ffn:
                    divide(b, C - 1)
                if att:
                    normalise1(b, C - 2)
                    low_x1(b, C - 2)
                if att and ffn:
                    divide(b, C - 1)
                if ffn:
                    norm2(f, 1)
                if att:
                    norm1(b, C - 1)
                if ffn:
                    norm2(f, 2)
                if att:
                    normalise1(b, C - 1)
                if ffn:
                    norm2(f, 3)
                if att:
                    low_x1(b, C - 1)

            def first_weights():
                dve.wait_ge(k0_in, 16)
                for g in range(G):
                    dve.tensor_tensor(w0[:, g, :], k0_raw[:, g, :], k0_raw[:, G + g, :],
                                      ALU.subtract).then_inc(scal, 1)
                dve.wait_ge(scal, 10)
                for g in range(G):
                    dve.tensor_scalar(w0[:, g, :], w0[:, g, :], c0[:], None, ALU.mult).then_inc(w0_ready, 1)

            dve.sem_inc(s_done.sem, 2)
            dve.memset(phi_eps[:], PHI_EPS).then_inc(scal, 1)
            dve.memset(vpad[:], 0.0).then_inc(zeroed, 1)
            dve.wait_ge(const_in, CONST_IN)
            dve.tensor_copy(blocks_r[:], blocks[:]).then_inc(blocks_ready, 1)
            dve.tensor_scalar(s_neg[:], s_raw[:], 0.0, None, ALU.is_lt).then_inc(scal, 1)
            dve.wait_ge(scal, 2)
            dve.scalar_tensor_tensor(out=s_sign[:], in0=s_raw[:], scalar=0.0, in1=s_neg[:], op0=ALU.is_gt,
                                     op1=ALU.subtract).then_inc(scal, 1)
            dve.wait_ge(scal, 3)
            dve.tensor_tensor(s_abs[:], s_raw[:], s_sign[:], ALU.mult).then_inc(scal, 1)
            dve.tensor_scalar(c1[:, 0:1], s_sign[:, 1:2], 2 * H2_SCALE / H1_SCALE, None,
                              ALU.mult).then_inc(scal, 1)
            dve.tensor_scalar(c1[:, 1:2], s_sign[:, 1:2], -H2_SCALE / H1_SCALE, None,
                              ALU.mult).then_inc(scal, 1)
            dve.tensor_scalar(c0[:], s_sign[:, 0:1], 2 * H1_SCALE / X_SCALE, None, ALU.mult).then_inc(scal, 1)
            dve.tensor_copy(ident16[:], ident[:]).then_inc(scal, 1)
            dve.wait_ge(scal, 4)
            dve.tensor_scalar(out_scale[:, 0:1], s_abs[:, 0:1], s_abs[:, 1:2], 4.0 / H2_SCALE, ALU.mult,
                              ALU.mult).then_inc(w0_ready, 1)
            dve.wait_ge(w0_ready, 1)
            dve.tensor_scalar(out_scale[:, 1:2], out_scale[:, 0:1], s_raw[:, 2:3], None,
                              ALU.mult).then_inc(w0_ready, 1)
            step(0, None, first_weights)
            with dve.Fori(0, B - 1) as f:
                step(f + 1, f)
            step(None, B - 1)

        @block.gpsimd
        def _(pool):
            def low_k(b, g):
                pool.wait_ge(k_high.sem, k_high.at(b, g + 1))
                pool.tensor_tensor(k_parts[:, 1, g, :], kf[:, g, :], k_parts[:, 0, g, :].bitcast(F32),
                                   ALU.subtract).then_inc(k_low.sem, 1)

            def times_prefix(b, g):
                pool.wait_ge(feat.sem, feat.at(b, G + g + 1))
                pool.wait_ge(scanned.sem, scanned.at(b, g + 1))
                pool.tensor_tensor(zc[:, g, :], qf[:, g, :], zc[:, g, :], ALU.mult).then_inc(qz_ready.sem, 1)

            def low_z(b, g):
                pool.wait_ge(z_high_ready.sem, z_high_ready.at(b, g + 1))
                pool.tensor_tensor(z_low[:, g, :], zc[:, g, :], z_high[:, g, :].bitcast(F32),
                                   ALU.subtract).then_inc(z_low_ready.sem, 1)

            def inverse_std1(b, c):
                pool.wait_ge(ln1_step.sem, ln1_step.at(b, 2 * c + 2))
                pool.tensor_tensor(rs1[:, c, 0:1], mv1[:, c, 1:2], consts[:, 0:1],
                                   ALU.add).then_inc(ln1_stat.sem, 1)
                pool.wait_ge(ln1_stat.sem, ln1_stat.at(b, 2 * c + 1))
                pool.tensor_tensor(rs1[:, c, 1:2], rs1[:, c, 0:1], consts[:, 1:2],
                                   ALU.pow).then_inc(ln1_stat.sem, 1)

            def inverse_std2(f, c):
                pool.wait_ge(ln2_step.sem, ln2_step.at(f, 2 * c + 2))
                pool.tensor_tensor(rs2[:, c, 0:1], mv2[:, c, 1:2], consts[:, 0:1],
                                   ALU.add).then_inc(ln2_stat.sem, 1)
                pool.tensor_tensor(rs2[:, c, 2:3], mv2[:, c, 0:1], consts[:, 2:3],
                                   ALU.mult).then_inc(ln2_stat.sem, 1)
                pool.wait_ge(ln2_stat.sem, ln2_stat.at(f, 4 * c + 1))
                pool.tensor_tensor(rs2[:, c, 1:2], rs2[:, c, 0:1], consts[:, 1:2],
                                   ALU.pow).then_inc(ln2_stat.sem, 1)
                pool.wait_ge(ln2_stat.sem, ln2_stat.at(f, 4 * c + 3))
                pool.tensor_tensor(rs2[:, c, 3:4], rs2[:, c, 2:3], rs2[:, c, 1:2],
                                   ALU.mult).then_inc(ln2_stat.sem, 1)

            def step(b, f):
                att, ffn = b is not None, f is not None
                if att:
                    for g in range(G):
                        low_k(b, g)
                    times_prefix(b, 0)
                    low_z(b, 0)
                    times_prefix(b, 1)
                    low_z(b, 1)
                    for c in range(C - 1):
                        inverse_std1(b, c)
                if ffn:
                    inverse_std2(f, 0)
                    inverse_std2(f, 1)
                if att:
                    inverse_std1(b, C - 1)
                if ffn:
                    for c in range(2, C):
                        inverse_std2(f, c)

            pool.memset(consts[:, 0:1], LN_EPS)
            pool.memset(consts[:, 2:3], -1.0)
            pool.memset(consts[:, 1:2], -0.5).then_inc(lnc_ready, 1)
            pool.wait_ge(lnc_ready, 1)
            pool.wait_ge(const_in, CONST_IN)
            step(0, None)
            with pool.Fori(0, B - 1) as f:
                step(f + 1, f)
            step(None, B - 1)


def kernel(L0_attn_x, L0_attn_Wq, L0_attn_Wk, L0_attn_Wv, L0_attn_Wo, L0_ffn_k0, L0_ffn_k1, L0_ffn_k2,
           L0_ffn_s0, L0_ffn_s1, L0_ffn_s2):
    import concourse.bacc as bacc
    from concourse.bass_utils import run_bass_kernel_spmd

    x = np.ascontiguousarray(L0_attn_x)
    p = np.arange(P)
    arrays = {
        "x": x,
        "x_t": np.ascontiguousarray(np.transpose(x, (0, 2, 1))),
        "wq_t": np.ascontiguousarray(np.transpose(L0_attn_Wq)),
        "wk_t": np.ascontiguousarray(np.transpose(L0_attn_Wk)),
        "wv_t": np.ascontiguousarray(np.transpose(L0_attn_Wv)),
        "wo_t": np.ascontiguousarray(np.transpose(L0_attn_Wo)),
        "k0": np.ascontiguousarray(L0_ffn_k0),
        "k1": np.ascontiguousarray(L0_ffn_k1),
        "k2": np.ascontiguousarray(L0_ffn_k2),
        "s": np.ascontiguousarray(np.broadcast_to(
            np.stack([np.asarray(L0_ffn_s0), np.asarray(L0_ffn_s1), np.asarray(L0_ffn_s2)])[None, :], (P, 3))),
        "causal": (p[:, None] <= p[None, :]).astype(np.float32),
        "blocks": (p[:, None] // DH == p[None, :] // DH).astype(np.float32),
        "ident": np.eye(P, dtype=np.float32),
        "parity": (p[:, None] // DH % 2 == np.arange(2)[None, :]).astype(np.float32),
    }
    nc = bacc.Bacc("TRN2", target_bir_lowering=False, num_devices=1)
    ins = [nc.dram_tensor(f"{n}_dram", a.shape, mybir.dt.from_np(a.dtype), kind="ExternalInput").ap()
           for n, a in arrays.items()]
    out = nc.dram_tensor("out_dram", (B, T, D), F32, kind="ExternalOutput").ap()
    layer_kernel(nc, *ins, out)
    r = run_bass_kernel_spmd(nc, [{f"{n}_dram": a for n, a in arrays.items()}], core_ids=[0])
    return r.results[0]["out_dram"]
```
